# Optimizing a Trainium2 kernel written in Bass

```python
import numpy as np
import jax
import jax.numpy as jnp

def _softmax(x, axis=-1):
    return jax.nn.softmax(x, axis=axis)

def _gelu(x):
    return jax.nn.gelu(x, approximate=True)

def _silu(x):
    return jax.nn.silu(x)

def _sigmoid(x):
    return jax.nn.sigmoid(x)

def _layernorm(x, axis=-1, eps=1e-05):
    m = jnp.mean(x, axis=axis, keepdims=True)
    v = jnp.var(x, axis=axis, keepdims=True)
    return (x - m) / jnp.sqrt(v + eps)

def _scatter_add(tgt, idx, src, axis=0):
    return tgt.at[idx].add(src)

def _segment_sum(src, seg, n):
    return jax.ops.segment_sum(src, seg, n)
kernel_name = 'mk_perceiver_d1_seqx_r2_795237'

def setup_inputs(seed: int=0):
    np.random.seed(seed)
    _w = jnp.asarray

    def _rec_inputs():
        import jax
        import jax.numpy as jnp
        _rk = jax.random.key(seed)
        x = -0.0002928 + 1 * jax.random.normal(jax.random.fold_in(_rk, 1), (2, 512, 512), jnp.float32)
        _lenS = 512 - jax.random.randint(jax.random.fold_in(_rk, 7), (2,), 0, max(1, 512 // 4) + 1, jnp.int32)
        _lenS2 = 8192 - jax.random.randint(jax.random.fold_in(_rk, 8), (2,), 0, max(1, 8192 // 4) + 1, jnp.int32)
        _ctx_1024P = jax.random.normal(jax.random.fold_in(_rk, 11), (2, 16, 512), jnp.float32)
        _ctx_1024c = jax.random.dirichlet(jax.random.fold_in(_rk, 511), 0.3 * jnp.ones((16,), jnp.float32), (2, 8192))
        _ctx_1024t = jnp.einsum('bsk,bkd->bsd', _ctx_1024c, _ctx_1024P)
        _ctx_1024t = _ctx_1024t * jax.lax.rsqrt(jnp.mean(jnp.square(_ctx_1024t)) + 1e-12) * 0.953939
        ctx_1024 = -1.39393e-06 + 0.999914 * (_ctx_1024t + 0.3 * jax.random.normal(jax.random.fold_in(_rk, 611), (2, 8192, 512), jnp.float32))
        _validS = jnp.arange(512)[None, :] < _lenS[:, None]
        _validS2 = jnp.arange(8192)[None, :] < _lenS2[:, None]
        _causal = jnp.tril(jnp.ones((512, 512), dtype=bool))
        mask_Bx1x1xS2_if1 = jnp.where(jnp.ones((2, 1, 1, 8192), dtype=bool), 1, 0).astype(jnp.int32)
        return (x, ctx_1024, mask_Bx1x1xS2_if1)
    x, ctx_1024, mask_Bx1x1xS2_if1 = _rec_inputs()

    def _L0_xattn_setup():
        import jax, jax.numpy as jnp
        import numpy as np
        N_HEADS = 16
        D_MODEL = 512
        D_K = D_MODEL // N_HEADS
        B, S = (2, 1024)
        key = jax.random.key(seed)
        ks = jax.random.split(key, 12)
        sc = 1.0 / np.sqrt(D_MODEL)
        inp = {'query': jax.random.normal(ks[0], (B, S, D_MODEL), jnp.float32), 'key': jax.random.normal(ks[1], (B, S, D_MODEL), jnp.float32), 'value': jax.random.normal(ks[2], (B, S, D_MODEL), jnp.float32), 'mask': jnp.ones((B, 1, 1, S), jnp.int32), 'Wq': jax.random.normal(ks[3], (D_MODEL, D_MODEL), jnp.float32) * sc, 'bq': jnp.zeros((D_MODEL,), jnp.float32), 'Wk': jax.random.normal(ks[4], (D_MODEL, D_MODEL), jnp.float32) * sc, 'bk': jnp.zeros((D_MODEL,), jnp.float32), 'Wv': jax.random.normal(ks[5], (D_MODEL, D_MODEL), jnp.float32) * sc, 'bv': jnp.zeros((D_MODEL,), jnp.float32), 'Wo': jax.random.normal(ks[6], (D_MODEL, D_MODEL), jnp.float32) * sc, 'bo': jnp.zeros((D_MODEL,), jnp.float32)}
        return inp
    _L0_xattn_all = _L0_xattn_setup()
    _L0_xattn_in = {k: v for k, v in _L0_xattn_all.items() if k in ('Wq', 'bq', 'Wk', 'bk', 'Wv', 'bv', 'Wo', 'bo')}
    del _L0_xattn_all

    def _L0_attn_setup():
        import jax, jax.numpy as jnp
        import numpy as np
        NUM_HEADS = 16
        WINDOW = 7

        def _window_indices(seq_len, window):
            half = window // 2
            idx = np.zeros((seq_len, window), dtype=np.int32)
            for i in range(seq_len):
                start = max(0, i - half)
                end = min(seq_len, i + half + 1)
                win = np.arange(start, end, dtype=np.int32)
                pad = window - len(win)
                if pad > 0:
                    if start == 0:
                        win = np.concatenate([win, np.full(pad, seq_len - 1, dtype=np.int32)])
                    else:
                        win = np.concatenate([np.zeros(pad, dtype=np.int32), win])
                idx[i] = win
            return jnp.asarray(idx)
        key = jax.random.key(seed)
        ks = jax.random.split(key, 7)
        B, S, E = (4, 1024, 512)
        D = E // NUM_HEADS
        s_e = 1.0 / np.sqrt(E)
        s_d = 1.0 / np.sqrt(D)
        return {'x': jax.random.normal(ks[0], (B, S, E), jnp.float32), 'W_qkv': jax.random.normal(ks[1], (3 * E, E), jnp.float32) * s_e, 'b_qkv': jnp.zeros((3 * E,), jnp.float32), 'W_lat': jax.random.normal(ks[2], (D, D), jnp.float32) * s_d, 'b_lat': jnp.zeros((D,), jnp.float32), 'W_proj': jax.random.normal(ks[3], (E, E), jnp.float32) * s_e, 'b_proj': jnp.zeros((E,), jnp.float32)}
    _L0_attn_all = _L0_attn_setup()
    _L0_attn_in = {k: v for k, v in _L0_attn_all.items() if k in ('W_qkv', 'b_qkv', 'W_lat', 'b_lat', 'W_proj', 'b_proj')}
    del _L0_attn_all

    def _L0_ffn_setup():
        import jax, jax.numpy as jnp
        import numpy as np
        import math
        E = 16
        TOP_K = 2
        D = 512
        F = 2048
        SH = 1024
        key = jax.random.key(seed)
        ks = jax.random.split(key, 10)
        s = lambda k, shape, fan: jax.random.normal(k, shape, jnp.float32) / np.sqrt(fan)
        return {'x': jax.random.normal(ks[0], (32, 128, D), jnp.float32), 'gate_w': s(ks[1], (E, D), D), 'up_w': s(ks[2], (E, F, D), D), 'up_b': s(ks[3], (E, F), D), 'gw': s(ks[4], (E, F, D), D), 'gb': s(ks[5], (E, F), D), 'down_w': s(ks[6], (E, D, F), F), 'down_b': s(ks[7], (E, D), F), 'sh_gate_w': s(ks[8], (SH, D), D), 'sh_up_w': s(ks[9], (SH, D), D), 'sh_down_w': s(jax.random.fold_in(key, 11), (D, SH), SH)}
    _L0_ffn_all = _L0_ffn_setup()
    _L0_ffn_in = {k: v for k, v in _L0_ffn_all.items() if k in ('gate_w', 'up_w', 'up_b', 'gw', 'gb', 'down_w', 'down_b', 'sh_gate_w', 'sh_up_w', 'sh_down_w')}
    del _L0_ffn_all
    return {'x': x, 'ctx_1024': ctx_1024, 'mask_Bx1x1xS2_if1': mask_Bx1x1xS2_if1, 'L0_xattn_Wq': _L0_xattn_in['Wq'], 'L0_xattn_bq': _L0_xattn_in['bq'], 'L0_xattn_Wk': _L0_xattn_in['Wk'], 'L0_xattn_bk': _L0_xattn_in['bk'], 'L0_xattn_Wv': _L0_xattn_in['Wv'], 'L0_xattn_bv': _L0_xattn_in['bv'], 'L0_xattn_Wo': _L0_xattn_in['Wo'], 'L0_xattn_bo': _L0_xattn_in['bo'], 'L0_attn_W_qkv': _L0_attn_in['W_qkv'], 'L0_attn_b_qkv': _L0_attn_in['b_qkv'], 'L0_attn_W_lat': _L0_attn_in['W_lat'], 'L0_attn_b_lat': _L0_attn_in['b_lat'], 'L0_attn_W_proj': _L0_attn_in['W_proj'], 'L0_attn_b_proj': _L0_attn_in['b_proj'], 'L0_ffn_gate_w': _L0_ffn_in['gate_w'], 'L0_ffn_up_w': _L0_ffn_in['up_w'], 'L0_ffn_up_b': _L0_ffn_in['up_b'], 'L0_ffn_gw': _L0_ffn_in['gw'], 'L0_ffn_gb': _L0_ffn_in['gb'], 'L0_ffn_down_w': _L0_ffn_in['down_w'], 'L0_ffn_down_b': _L0_ffn_in['down_b'], 'L0_ffn_sh_gate_w': _L0_ffn_in['sh_gate_w'], 'L0_ffn_sh_up_w': _L0_ffn_in['sh_up_w'], 'L0_ffn_sh_down_w': _L0_ffn_in['sh_down_w']}

def reference(x, ctx_1024, mask_Bx1x1xS2_if1, L0_xattn_Wq, L0_xattn_bq, L0_xattn_Wk, L0_xattn_bk, L0_xattn_Wv, L0_xattn_bv, L0_xattn_Wo, L0_xattn_bo, L0_attn_W_qkv, L0_attn_b_qkv, L0_attn_W_lat, L0_attn_b_lat, L0_attn_W_proj, L0_attn_b_proj, L0_ffn_gate_w, L0_ffn_up_w, L0_ffn_up_b, L0_ffn_gw, L0_ffn_gb, L0_ffn_down_w, L0_ffn_down_b, L0_ffn_sh_gate_w, L0_ffn_sh_up_w, L0_ffn_sh_down_w):
    import jax
    import jax.numpy as jnp

    def _L0_xattn_ref(query, key, value, mask, Wq, bq, Wk, bk, Wv, bv, Wo, bo):
        import jax, jax.numpy as jnp
        import numpy as np
        N_HEADS = 16
        D_MODEL = 512
        D_K = D_MODEL // N_HEADS
        B, S = (2, 1024)
        q = query @ Wq.T + bq
        k = key @ Wk.T + bk
        v = value @ Wv.T + bv

        def split_heads(x):
            b, s, _ = x.shape
            return x.reshape(b, s, N_HEADS, D_K).transpose(0, 2, 1, 3)
        q, k, v = (split_heads(q), split_heads(k), split_heads(v))
        att = jnp.einsum('bhqd,bhkd->bhqk', q, k) / jnp.sqrt(jnp.float32(D_K))
        att = jnp.where(mask == 0, -jnp.inf, att)
        scores = jax.nn.softmax(att, axis=-1)
        out = jnp.einsum('bhqk,bhkd->bhqd', scores, v)
        b = out.shape[0]
        out = out.transpose(0, 2, 1, 3).reshape(b, -1, N_HEADS * D_K)
        return out @ Wo.T + bo

    def _L0_attn_ref(x, W_qkv, b_qkv, W_lat, b_lat, W_proj, b_proj):
        import jax, jax.numpy as jnp
        import numpy as np
        NUM_HEADS = 16
        WINDOW = 7

        def _window_indices(seq_len, window):
            half = window // 2
            idx = np.zeros((seq_len, window), dtype=np.int32)
            for i in range(seq_len):
                start = max(0, i - half)
                end = min(seq_len, i + half + 1)
                win = np.arange(start, end, dtype=np.int32)
                pad = window - len(win)
                if pad > 0:
                    if start == 0:
                        win = np.concatenate([win, np.full(pad, seq_len - 1, dtype=np.int32)])
                    else:
                        win = np.concatenate([np.zeros(pad, dtype=np.int32), win])
                idx[i] = win
            return jnp.asarray(idx)
        B, S, E = x.shape
        H = NUM_HEADS
        D = E // H
        qkv = (x @ W_qkv.T + b_qkv).reshape(B, S, 3, H, D).transpose(2, 0, 3, 1, 4)
        q, k, v = (qkv[0], qkv[1], qkv[2])
        k_lat = k @ W_lat.T + b_lat
        v_lat = v @ W_lat.T + b_lat
        widx = _window_indices(S, WINDOW)
        kw = k_lat[:, :, widx, :]
        vw = v_lat[:, :, widx, :]
        scale = 1.0 / np.sqrt(D)
        attn = jnp.einsum('bhsd,bhswd->bhsw', q, kw) * scale
        attn = jax.nn.softmax(attn, axis=-1)
        out = jnp.einsum('bhsw,bhswd->bhsd', attn, vw)
        out = out.transpose(0, 2, 1, 3).reshape(B, S, E)
        return out @ W_proj.T + b_proj

    def _L0_ffn_ref(x, gate_w, up_w, up_b, gw, gb, down_w, down_b, sh_gate_w, sh_up_w, sh_down_w):
        import jax, jax.numpy as jnp
        import numpy as np
        import math
        E = 16
        TOP_K = 2
        D = 512
        F = 2048
        SH = 1024
        B, S, Dm = x.shape
        h = x.reshape(-1, Dm)
        T = h.shape[0]
        scores = jax.nn.sigmoid(h @ gate_w.T)
        cap = math.ceil(T / E * TOP_K)
        topk_score, topk_ids = jax.lax.top_k(scores.T, cap)
        xin = h[topk_ids]
        up = jnp.einsum('ecd,efd->ecf', xin, up_w) + up_b[:, None, :]
        g = jnp.einsum('ecd,efd->ecf', xin, gw) + gb[:, None, :]
        eo = jax.nn.silu(g) * up
        eo = jnp.einsum('ecf,edf->ecd', eo, down_w) + down_b[:, None, :]
        flat = (eo * topk_score[..., None]).reshape(-1, Dm)
        out = jnp.zeros_like(h).at[topk_ids.reshape(-1)].add(flat)
        out = out.reshape(B, S, Dm)
        shared = jax.nn.silu(jnp.einsum('bsd,fd->bsf', x, sh_gate_w)) * jnp.einsum('bsd,fd->bsf', x, sh_up_w)
        shared = jnp.einsum('bsf,df->bsd', shared, sh_down_w)
        return out + shared
    x = x + _L0_xattn_ref(_layernorm(x, axis=-1), ctx_1024, ctx_1024, mask_Bx1x1xS2_if1, L0_xattn_Wq, L0_xattn_bq, L0_xattn_Wk, L0_xattn_bk, L0_xattn_Wv, L0_xattn_bv, L0_xattn_Wo, L0_xattn_bo)
    x = x + _L0_attn_ref(_layernorm(x, axis=-1), L0_attn_W_qkv, L0_attn_b_qkv, L0_attn_W_lat, L0_attn_b_lat, L0_attn_W_proj, L0_attn_b_proj)
    x = x + _L0_ffn_ref(_layernorm(x, axis=-1), L0_ffn_gate_w, L0_ffn_up_w, L0_ffn_up_b, L0_ffn_gw, L0_ffn_gb, L0_ffn_down_w, L0_ffn_down_b, L0_ffn_sh_gate_w, L0_ffn_sh_up_w, L0_ffn_sh_down_w)
    return x

_drawn_inputs = setup_inputs


def setup_inputs(seed=0):
    import zlib

    import numpy as np

    out = dict(_drawn_inputs(seed))
    spreads = {'L0_xattn_bq': (0.0, 0.1),
     'L0_xattn_bk': (0.0, 0.8),
     'L0_xattn_bv': (0.0, 0.1),
     'L0_xattn_bo': (0.0, 0.1),
     'L0_attn_b_qkv': (0.0, 0.1),
     'L0_attn_b_lat': (0.0, 0.1),
     'L0_attn_b_proj': (0.0, 0.1)}
    factors = {'L0_ffn_up_b': 3.107, 'L0_ffn_gb': 3.02, 'L0_ffn_down_b': 3.745}
    for name, (base, spread) in spreads.items():
        noise = np.random.default_rng([zlib.crc32(name.encode()), seed]).standard_normal(out[name].shape)
        drawn = base * np.exp(spread * noise) if base else spread * noise
        out[name] = jnp.asarray(drawn.astype(out[name].dtype))
    for name, factor in factors.items():
        out[name] = (out[name] * factor).astype(out[name].dtype)
    return out
```

```python
from contextlib import ExitStack

import numpy as np

import concourse.bass as bass
from concourse import mybir

F32 = mybir.dt.float32
F32R = mybir.dt.float32r
I32 = mybir.dt.int32
U32 = mybir.dt.uint32
ALU = mybir.AluOpType
ACT = mybir.ActivationFunctionType
AX = mybir.AxisListType

P = 128
B, SQ, D = 2, 512, 512
T = B * SQ
TT = T // P
H, DH = 16, 32
G = D // P
J = P // DH
DC = D // P
SK = 8192
CK = 512
NCH = SK // CK
KT = CK // P
BG = B * G
HALF = 3
EPS = 1e-5
SCALE = DH ** -0.5
BOUND = 60.0
MASKED = -1e30
E, FF, CAP = 16, 2048, 128
SH = 1024


class Chain:

    def __init__(self, engine, sem):
        self.engine, self.sem, self.count = engine, sem, 0

    def mark(self, instruction):
        self.count += 1
        instruction.then_inc(self.sem, 1)
        return self.count

    def link(self, instruction):
        self.engine.wait_ge(self.sem, self.mark(instruction))


def program(nc, x, ctx_t, mask, wq, bq, wk, bk, wv, bv, ident_d, blocks_d, wo, bo, wqkv, bqkv, wlat, blat_c,
            blat_r, wmask_d, wproj, bproj, gate_w, up_w, up_b, gw, gb, down_w, down_b, sh_gate, sh_up, sh_down, out):
    st = ExitStack()
    with st:
        def sem(name):
            return st.enter_context(nc.semaphore(name))

        def dram(name, shape, dt):
            return nc.dram_tensor(name, shape, dt).ap()

        qh_d = dram("qh_d", [BG, P, SQ], F32)
        ql_d = dram("ql_d", [BG, P, SQ], F32)
        shift_d = dram("shift_d", [2, BG * J, SQ], F32)
        kh_d = dram("kh_d", [B * NCH, G, P, CK], F32)
        kl_d = dram("kl_d", [B * NCH, G, P, CK], F32)
        v_d = dram("v_d", [B * NCH, G, P, KT, P], F32)
        mask_d = dram("mask_d", [B * NCH, CK], F32)

        PS = st.enter_context(nc.psum_tensor("PS", [P, 8, 512], F32))
        X = st.enter_context(nc.sbuf_tensor("X", [P, TT, D], F32))
        ident = st.enter_context(nc.sbuf_tensor("ident", [P, P], F32))
        ones = st.enter_context(nc.sbuf_tensor("ones", [P, DH], F32))
        qn2 = st.enter_context(nc.sbuf_tensor("qn2", [P, BG], F32))
        kmax = st.enter_context(nc.sbuf_tensor("kmax", [P, B * NCH, G], F32))
        blocks = st.enter_context(nc.sbuf_tensor("blocks", [P, P], F32))
        flag = st.enter_context(nc.sbuf_tensor("flag", [1, 1], I32))

        s_var, s_root = sem("variance_ready"), sem("root_ready")

        def emit_root(act, tmp, k):
            act.wait_ge(s_var, k)
            nc.scalar.activation(tmp[:, :, 9], tmp[:, :, 8], ACT.Sqrt).then_inc(s_root, 1)

        def emit_layernorm(chain, src, dst, tmp, ready, k):
            v = nc.vector
            for i in range(TT):
                n = chain.mark(v.bn_stats(tmp[:, i, 0:6], src[:, i, :]))
            chain.engine.wait_ge(chain.sem, n)
            for i in range(TT):
                n = chain.mark(v.bn_aggr(tmp[:, i, 6:8], tmp[:, i, 0:6]))
            chain.engine.wait_ge(chain.sem, n)
            v.tensor_scalar(tmp[:, :, 8], tmp[:, :, 7], EPS, None, ALU.add).then_inc(s_var, 1)
            chain.engine.wait_ge(s_root, k)
            chain.link(v.reciprocal(tmp[:, :, 10], tmp[:, :, 9]))
            chain.link(v.tensor_tensor(tmp[:, :, 11], tmp[:, :, 8], tmp[:, :, 10], ALU.mult))
            chain.link(v.tensor_tensor(tmp[:, :, 12], tmp[:, :, 11], tmp[:, :, 10], ALU.mult))
            chain.link(v.tensor_scalar(tmp[:, :, 13], tmp[:, :, 12], -0.5, 1.5, ALU.mult, ALU.add))
            chain.link(v.tensor_tensor(tmp[:, :, 14], tmp[:, :, 13], tmp[:, :, 10], ALU.mult))
            for i in range(TT):
                v.tensor_scalar(dst[:, i, :], src[:, i, :], tmp[:, i, 6:7], tmp[:, i, 14:15],
                                ALU.subtract, ALU.mult).then_inc(ready, 1)

        proj = ExitStack()
        with proj:
            def wt(name):
                return proj.enter_context(nc.sbuf_tensor(name, [P, DC, D], F32R))

            WKH, WKL, WVH, WVL = wt("WKH"), wt("WKL"), wt("WVH"), wt("WVL")
            bk_s = proj.enter_context(nc.sbuf_tensor("bk_s", [P, G], F32))
            bv_s = proj.enter_context(nc.sbuf_tensor("bv_s", [P, D], F32))

            s_x, s_wq, s_wk, s_wv, s_small, s_mask = (sem(n) for n in (
                "x_in", "wq_in", "wk_in", "wv_in", "small_in", "mask_in"))
            s_xn, s_tp, s_xt = sem("xn_ready"), sem("turned_ready"), sem("xt_ready")
            s_q, s_qh, s_ql, s_sq, s_nrm, s_nmax = (sem(n) for n in (
                "q_ready", "q_hi_ready", "q_lo_ready", "q_square_ready", "q_norm_ready", "q_norm_max"))
            s_whi, s_qst = sem("w_hi_ready"), [sem(f"q_stored{i}") for i in range(2)]
            s_rows, s_rowst, s_dch, s_bl = sem("rows_ready"), sem("rows_stored"), sem("dve_chain1"), sem("blocks_ready")
            with ExitStack() as s1, nc.Block() as block:
                def sb(name, shape, dt=F32):
                    return s1.enter_context(nc.sbuf_tensor(name, shape, dt))

                XN = sb("XN", [P, TT, D])
                XT = sb("XT", [P, DC, T])
                WQ, WK, WV = sb("WQ", [P, DC, D]), sb("WK", [P, DC, D]), sb("WV", [P, DC, D])
                bq_s = sb("bq_s", [P, G])
                tmp = sb("ln_tmp", [P, TT, 15])
                QH, QL = sb("QH", [P, 2, SQ], F32R), sb("QL", [P, 2, SQ], F32R)
                QQ = sb("QQ", [P, 2, SQ])
                MI = sb("MI", [B * NCH, CK], I32)
                MR = sb("MR", [B * NCH, CK], F32R)
                RO = sb("RO", [BG * J, SQ], F32R)
                RZ = sb("RZ", [BG * J, SQ], F32R)

                @block.sync
                def _(sp):
                    sp.dma_start(X[:], x.rearrange("(i p) d -> p i d", p=P)).then_inc(s_x, 16)
                    sp.dma_start(ident[:], ident_d).then_inc(s_small, 16)
                    sp.dma_start(blocks[:], blocks_d).then_inc(s_small, 16)
                    sp.dma_start(bq_s[:], bq).then_inc(s_small, 16)
                    sp.dma_start(bk_s[:], bk).then_inc(s_small, 16)
                    sp.dma_start(bv_s[:], bv.partition_broadcast(P)).then_inc(s_small, 16)
                    sp.dma_start(MI[:], mask).then_inc(s_mask, 16)
                    sp.dma_start(WQ[:], wq).then_inc(s_wq, 16)
                    sp.dma_start(WK[:], wk).then_inc(s_wk, 16)
                    sp.dma_start(WV[:], wv).then_inc(s_wv, 16)
                    sp.wait_ge(s_rows, 3)
                    sp.dma_start(shift_d[0], RZ[:].bitcast(F32)).then_inc(s_rowst, 16)
                    sp.dma_start(shift_d[1], RO[:].bitcast(F32)).then_inc(s_rowst, 16)
                    sp.dma_start(mask_d, MR[:].bitcast(F32)).then_inc(s_rowst, 16)
                    for n in range(BG):
                        sp.wait_ge(s_qh, n + 1)
                        sp.dma_start(qh_d[n], QH[:, n % 2, :].bitcast(F32)).then_inc(s_qst[n % 2], 16)
                        sp.wait_ge(s_ql, n + 1)
                        sp.dma_start(ql_d[n], QL[:, n % 2, :].bitcast(F32)).then_inc(s_qst[n % 2], 16)
                    sp.wait_ge(s_rowst, 16 * 3)
                    for i in range(2):
                        sp.wait_ge(s_qst[i], 32 * (BG // 2))

                @block.vector
                def _(dve):
                    v = nc.vector
                    chain = Chain(dve, s_dch)
                    v.memset(ones[:], 1.0)
                    v.memset(RZ[:].bitcast(F32), 0.0).then_inc(s_rows, 1)
                    v.memset(RO[:].bitcast(F32), 1.0).then_inc(s_rows, 1)
                    dve.wait_ge(s_mask, 16)
                    v.tensor_scalar(MR[:], MI[:], 0, MASKED, ALU.is_equal, ALU.mult).then_inc(s_rows, 1)
                    dve.wait_ge(s_x, 16)
                    emit_layernorm(chain, X, XN, tmp, s_xn, 1)
                    dve.wait_ge(s_small, 80)
                    dve.wait_ge(s_whi, 2)
                    for i in range(TT):
                        if i == TT - 2:
                            v.tensor_tensor(WKL[:], WK[:], WKH[:].bitcast(F32), ALU.subtract)
                            v.tensor_tensor(WVL[:], WV[:], WVH[:].bitcast(F32), ALU.subtract)
                        dve.wait_ge(s_tp, i + 1)
                        v.tensor_copy(XT[:, :, i * P:(i + 1) * P],
                                      PS[:, i % 2, :].rearrange("p (c t) -> p c t", c=DC)).then_inc(s_xt, 1)

                    def largest(n):
                        dve.wait_ge(s_nrm, n + 1)
                        v.tensor_reduce(qn2[:, n:n + 1], PS[:, 4 + n % 2, :], AX.X, ALU.max).then_inc(s_nmax, 1)

                    for n in range(BG):
                        g = n % G
                        dve.wait_ge(s_q, n + 1)
                        dve.wait_ge(s_qh, n + 1)
                        if n >= 2:
                            dve.wait_ge(s_qst[n % 2], 32 * (n // 2))
                        v.scalar_tensor_tensor(QL[:, n % 2, :], PS[:, 2 + n % 2, :], bq_s[:, g:g + 1],
                                               QH[:, n % 2, :].bitcast(F32), ALU.add, ALU.subtract).then_inc(s_ql, 1)
                        if n:
                            largest(n - 1)
                    largest(BG - 1)

                @block.scalar
                def _(act):
                    emit_root(act, tmp, 1)
                    act.wait_ge(s_wk, 16)
                    nc.scalar.activation(WKH[:], WK[:], ACT.Copy).then_inc(s_whi, 1)
                    act.wait_ge(s_wv, 16)
                    nc.scalar.activation(WVH[:], WV[:], ACT.Copy).then_inc(s_whi, 1)
                    act.wait_ge(s_small, 80)
                    for n in range(BG):
                        g = n % G
                        act.wait_ge(s_q, n + 1)
                        if n >= 2:
                            act.wait_ge(s_qst[n % 2], 32 * (n // 2))
                            act.wait_ge(s_nrm, n - 1)
                        nc.scalar.activation(QH[:, n % 2, :], PS[:, 2 + n % 2, :], ACT.Identity,
                                             bias=bq_s[:, g:g + 1]).then_inc(s_qh, 1)
                        act.wait_ge(s_qh, n + 1)
                        nc.scalar.activation(QQ[:, n % 2, :], QH[:, n % 2, :].bitcast(F32), ACT.Square).then_inc(s_sq, 1)

                @block.tensor
                def _(pe):
                    pe.wait_ge(s_small, 80)
                    for i in range(TT):
                        pe.wait_ge(s_xn, i + 1)
                        if i >= 2:
                            pe.wait_ge(s_xt, i - 1)
                        for c in range(DC):
                            m = pe.transpose(PS[:, i % 2, c * P:(c + 1) * P], XN[:, i, c * P:(c + 1) * P], ident[:])
                        m.then_inc(s_tp, 1)
                    def norms(n):
                        pe.wait_ge(s_sq, n + 1)
                        if n >= 2:
                            pe.wait_ge(s_nmax, n - 1)
                        pe.matmul(PS[:, 4 + n % 2, :], blocks[:], QQ[:, n % 2, :], start=True, stop=True).then_inc(s_nrm, 1)

                    pe.wait_ge(s_wq, 16)
                    for n in range(BG):
                        b, g = divmod(n, G)
                        pe.wait_ge(s_xt, (b + 1) * TT // B)
                        if n >= 2:
                            pe.wait_ge(s_ql, n - 1)
                            pe.wait_ge(s_sq, n - 1)
                        for c in range(DC):
                            m = pe.matmul(PS[:, 2 + n % 2, :], WQ[:, c, g * P:(g + 1) * P],
                                          XT[:, c, b * SQ:(b + 1) * SQ], start=(c == 0), stop=(c == DC - 1))
                        m.then_inc(s_q, 1)
                        if n:
                            norms(n - 1)
                    norms(BG - 1)

            s_cx = [sem(f"ctx_in{i}") for i in range(2)]
            s_chi, s_clo = sem("ctx_hi_ready"), sem("ctx_lo_ready")
            s_kps, s_vps, s_kh, s_kl, s_vs = (sem(n) for n in (
                "k_psum_ready", "v_psum_ready", "k_hi_ready", "k_lo_ready", "v_ready"))
            s_kvst = [sem(f"kv_stored{i}") for i in range(2)]
            STORES = 16 * (2 + G)
            with ExitStack() as s2, nc.Block() as block:
                def sb(name, shape, dt=F32):
                    return s2.enter_context(nc.sbuf_tensor(name, shape, dt))

                CX = [sb(f"CX{i}", [P, DC, CK]) for i in range(2)]
                CH = [sb(f"CH{i}", [P, DC, CK], F32R) for i in range(2)]
                CL = [sb(f"CL{i}", [P, DC, CK], F32R) for i in range(2)]
                KH = [sb(f"KH{i}", [P, G, CK], F32R) for i in range(2)]
                KL = [sb(f"KL{i}", [P, G, CK], F32R) for i in range(2)]
                VS = [sb(f"VS{i}", [P, KT, D]) for i in range(2)]

                @block.sync
                def _(sp):
                    def pair(i, last=False):
                        for s in range(2):
                            n = i * 2 + s
                            if not (last and s == 1):
                                sp.wait_ge(s_clo, n + 2)
                                sp.dma_start(CX[1 - s][:], ctx_t[n + 1]).then_inc(s_cx[1 - s], 16)
                            sp.wait_ge(s_kh, n * G + G)
                            sp.dma_start(kh_d[n].rearrange("g p k -> p g k"), KH[s][:].bitcast(F32)).then_inc(s_kvst[s], 16)
                            sp.wait_ge(s_kl, n * G + 2 * G)
                            sp.dma_start(kl_d[n].rearrange("g p k -> p g k"), KL[s][:].bitcast(F32)).then_inc(s_kvst[s], 16)
                            sp.wait_ge(s_vs, n * KT + 2 * KT)
                            for g in range(G):
                                sp.dma_start(v_d[n, g], VS[s][:, :, g * P:(g + 1) * P]).then_inc(s_kvst[s], 16)

                    for s in range(2):
                        sp.sem_inc(s_kvst[s], 1)
                    sp.dma_start(CX[0][:], ctx_t[0]).then_inc(s_cx[0], 16)
                    with sp.Fori(0, B * NCH // 2 - 1) as i:
                        pair(i)
                    pair(B * NCH // 2 - 1, last=True)
                    for s in range(2):
                        sp.wait_ge(s_kvst[s], STORES * B * NCH // 2 + 1)

                @block.scalar
                def _(act):
                    def split(n, m, s):
                        act.wait_ge(s_cx[s], m * 16 + 16)
                        act.wait_ge(s_vps, n * KT + KT)
                        nc.scalar.activation(CH[s][:], CX[s][:], ACT.Copy).then_inc(s_chi, 1)

                    def pair(m, last=False):
                        for s in range(2):
                            n = m * 2 + s
                            act.wait_ge(s_kvst[s], m * STORES + 1)
                            for g in range(G):
                                act.wait_ge(s_kps, n * G + g + 1)
                                nc.scalar.activation(KH[s][:, g, :], PS[:, g, :], ACT.Identity,
                                                     bias=bk_s[:, g:g + 1]).then_inc(s_kh, 1)
                                if g == 1 and not (last and s == 1):
                                    split(n + 1, m + s, 1 - s)

                    split(0, 0, 0)
                    with act.Fori(0, B * NCH // 2 - 1) as m:
                        pair(m)
                    pair(B * NCH // 2 - 1, last=True)

                @block.vector
                def _(dve):
                    v = nc.vector

                    def split(n, s):
                        dve.wait_ge(s_chi, n + 1)
                        v.tensor_tensor(CL[s][:], CX[s][:], CH[s][:].bitcast(F32), ALU.subtract).then_inc(s_clo, 1)

                    def pair(m, last=False):
                        for s in range(2):
                            n = m * 2 + s
                            dve.wait_ge(s_kvst[s], m * STORES + 1)
                            for g in range(G):
                                dve.wait_ge(s_kh, n * G + g + 1)
                                v.scalar_tensor_tensor(KL[s][:, g, :], PS[:, g, :], bk_s[:, g:g + 1],
                                                       KH[s][:, g, :].bitcast(F32), ALU.add, ALU.subtract).then_inc(s_kl, 1)
                            if not (last and s == 1):
                                split(n + 1, 1 - s)
                            v.tensor_reduce(kmax[:, n, :], KH[s][:].bitcast(F32), AX.X, ALU.max,
                                            apply_absolute_value=True)
                            for t in range(KT):
                                dve.wait_ge(s_vps, n * KT + 2 * KT + t + 1)
                                v.tensor_tensor(VS[s][:, t, :], PS[:, G + t, :], bv_s[:], ALU.add).then_inc(s_vs, 1)

                    dve.sem_inc(s_clo, 2)
                    dve.sem_inc(s_kl, G)
                    dve.sem_inc(s_vs, KT)
                    split(0, 0)
                    with dve.Fori(0, B * NCH // 2 - 1) as m:
                        pair(m)
                    pair(B * NCH // 2 - 1, last=True)

                @block.tensor
                def _(pe):
                    pe.sem_inc(s_vps, 2 * KT)
                    with pe.Fori(0, B * NCH // 2) as m:
                        for s in range(2):
                            n = m * 2 + s
                            pe.wait_ge(s_clo, n + 3)
                            for g in range(G):
                                pe.wait_ge(s_kl, n * G + g + 1)
                                terms = [(w, a, c) for c in range(DC) for w, a in ((WKH, CH), (WKH, CL), (WKL, CH))]
                                for k, (w, a, c) in enumerate(terms):
                                    mm = pe.matmul(PS[:, g, :], w[:, c, g * P:(g + 1) * P], a[s][:, c, :],
                                                   start=(k == 0), stop=(k == len(terms) - 1))
                                mm.then_inc(s_kps, 1)
                            for t in range(KT):
                                pe.wait_ge(s_vs, n * KT + t + 1)
                                terms = [(a, w, c) for c in range(DC) for a, w in ((CH, WVH), (CH, WVL), (CL, WVH))]
                                for k, (a, w, c) in enumerate(terms):
                                    mm = pe.matmul(PS[:, G + t, :], a[s][:, c, t * P:(t + 1) * P], w[:, c, :],
                                                   start=(k == 0), stop=(k == len(terms) - 1))
                                mm.then_inc(s_vps, 1)


        s_b, s_bp = sem("bound_step"), sem("bound_product")
        with ExitStack() as s3, nc.Block() as block:
            kx = s3.enter_context(nc.sbuf_tensor("kx", [P, 4, BG], F32))

            @block.vector
            def _(dve):
                v = nc.vector
                chain = Chain(dve, s_b)
                for b in range(B):
                    n = chain.mark(v.tensor_reduce(kx[:, 0, b * G:(b + 1) * G],
                                                   kmax[:, b * NCH:(b + 1) * NCH, :].rearrange("p c g -> p g c"), AX.X, ALU.max))
                dve.wait_ge(s_b, n)
                chain.link(v.tensor_tensor(kx[:, 1, :], kx[:, 0, :], kx[:, 0, :], ALU.mult))
                dve.wait_ge(s_bp, 1)
                chain.link(v.tensor_tensor(kx[:, 2, :], PS[:, 0, 0:BG], qn2[:], ALU.mult))
                chain.link(v.tensor_reduce(kx[:, 3, 0:1], kx[:, 2, :], AX.X, ALU.max))
                dve.wait_ge(s_bp, 2)
                chain.link(v.tensor_reduce(kx[0:1, 3, 1:2], PS[0:1, 1, 0:P], AX.X, ALU.max))
                chain.link(v.tensor_scalar(flag[:], kx[0:1, 3, 1:2], (BOUND / SCALE) ** 2, None, ALU.is_le))

            @block.tensor
            def _(pe):
                pe.wait_ge(s_b, B + 1)
                pe.matmul(PS[:, 0, 0:BG], blocks[:], kx[:, 1, :], start=True, stop=True).then_inc(s_bp, 1)
                pe.wait_ge(s_b, B + 3)
                pe.transpose(PS[0:1, 1, 0:P], kx[:, 3, 0:1], ident[:]).then_inc(s_bp, 1)

        s_mq, s_mk, s_mps, s_mx, s_mst = (
            sem("max_q_in"), [sem(f"max_k_in{i}") for i in range(2)], sem("max_psum_ready"),
            sem("max_taken"), sem("max_stored"))
        s_mrow, s_mch, s_mr = sem("max_row_ready"), sem("max_merged"), sem("max_reduced")
        KK = TT // B * J
        with ExitStack() as s4, nc.Block() as block:
            QM = s4.enter_context(nc.sbuf_tensor("QM", [P, J, SQ], F32R))
            KC = [s4.enter_context(nc.sbuf_tensor(f"KC{i}", [P, CK], F32R)) for i in range(2)]
            MB = [s4.enter_context(nc.sbuf_tensor(f"MB{i}", [P, CK], F32)) for i in range(2)]
            JK = s4.enter_context(nc.sbuf_tensor("JK", [P, CK], F32))
            MX = [s4.enter_context(nc.sbuf_tensor(f"MX{i}", [P, KK], F32)) for i in range(2)]
            RM = s4.enter_context(nc.sbuf_tensor("RM", [P, KK], F32))
            NM = s4.enter_context(nc.sbuf_tensor("NM", [P, KK], F32R))

            @block.sync
            def _(sp):
                with sp.If(sp.value_load(flag[0:1, 0:1]) == 0):
                    sp.sem_inc(s_mst, 1)
                    with sp.Fori(0, B) as b:
                        with sp.Fori(0, G) as g:
                            sp.wait_ge(s_mrow, 1)
                            sp.wait_ge(s_mps, (b * G + g) * (NCH * KK) + 1)
                            for j in range(J):
                                sp.dma_start(QM[j * DH:(j + 1) * DH, j, :].bitcast(F32),
                                             qh_d[b * G + g, j * DH:(j + 1) * DH, :]).then_inc(s_mq, 16)
                            with sp.Fori(0, NCH // 2) as i:
                                for s in range(2):
                                    N = (b * G + g) * NCH + i * 2 + s
                                    sp.wait_ge(s_mx, N * KK + KK)
                                    sp.dma_start(KC[s][:].bitcast(F32), kh_d[b * NCH + i * 2 + s, g]).then_inc(s_mk[s], 16)
                                    sp.dma_start(MB[s][:], mask_d[b * NCH + i * 2 + s].partition_broadcast(P)).then_inc(s_mk[s], 16)
                            sp.wait_ge(s_mrow, b * G + g + 2)
                            for j in range(J):
                                for q in range(SQ // P):
                                    sp.dma_start(shift_d[0, (b * G + g) * J + j, q * P:(q + 1) * P],
                                                 NM[:, q * J + j:q * J + j + 1].bitcast(F32)).then_inc(s_mst, 16)
                    sp.wait_ge(s_mst, BG * KK * 16 + 1)

            @block.tensor
            def _(pe):
                with pe.If(pe.value_load(flag[0:1, 0:1]) == 0):
                    pe.sem_inc(s_mps, 1)
                    with pe.Fori(0, B) as b:
                        with pe.Fori(0, G) as g:
                            with pe.Fori(0, NCH // 2) as i:
                                for s in range(2):
                                    N = (b * G + g) * NCH + i * 2 + s
                                    pe.wait_ge(s_mq, (b * G + g) * (16 * J) + 16 * J)
                                    pe.wait_ge(s_mk[s], ((b * G + g) * (NCH // 2) + i) * 32 + 32)
                                    for k in range(KK):
                                        pe.wait_ge(s_mx, N * KK + 2 * KK - 8 + k + 1)
                                        q, j = divmod(k, J)
                                        pe.matmul(PS[:, k % 8, :], QM[:, j, q * P:(q + 1) * P], KC[s][:],
                                                  start=True, stop=True).then_inc(s_mps, 1)

            @block.vector
            def _(dve):
                v = nc.vector
                with dve.If(dve.value_load(flag[0:1, 0:1]) == 0):
                    dve.sem_inc(s_mx, 2 * KK)
                    dve.sem_inc(s_mr, 1)
                    v.memset(QM[:].bitcast(F32), 0.0).then_inc(s_mrow, 1)
                    with dve.Fori(0, B) as b:
                        with dve.Fori(0, G) as g:
                            dve.wait_ge(s_mrow, b * G + g + 1)
                            v.memset(RM[:], -3e38).then_inc(s_mch, 1)
                            with dve.Fori(0, NCH // 2) as i:
                                for s in range(2):
                                    N = (b * G + g) * NCH + i * 2 + s
                                    dve.wait_ge(s_mk[s], ((b * G + g) * (NCH // 2) + i) * 32 + 32)
                                    dve.wait_ge(s_mch, (b * G + g) * (NCH + 1) + i * 2 + s + 1)
                                    for k in range(KK):
                                        dve.wait_ge(s_mps, N * KK + k + 2)
                                        dve.wait_ge(s_mr, N * KK + k + 1)
                                        v.tensor_tensor(JK[:], PS[:, k % 8, :], MB[s][:], ALU.add).then_inc(s_mx, 1)
                                        dve.wait_ge(s_mx, N * KK + 2 * KK + k + 1)
                                        v.tensor_reduce(MX[s][:, k:k + 1], JK[:], AX.X, ALU.max).then_inc(s_mr, 1)
                                    dve.wait_ge(s_mr, N * KK + KK + 1)
                                    v.tensor_tensor(RM[:], RM[:], MX[s][:], ALU.max).then_inc(s_mch, 1)
                            dve.wait_ge(s_mch, (b * G + g) * (NCH + 1) + NCH + 1)
                            dve.wait_ge(s_mst, (b * G + g) * (16 * KK) + 1)
                            v.tensor_scalar(NM[:], RM[:], -1.0, None, ALU.mult).then_inc(s_mrow, 1)

        AT = st.enter_context(nc.sbuf_tensor("AT", [P, BG, SQ], F32))
        six = ExitStack()
        WO = six.enter_context(nc.sbuf_tensor("WO", [P, G, D], F32))
        BO = six.enter_context(nc.sbuf_tensor("BO", [P, D], F32))
        s_wo = sem("output_weights_in")
        s_qs = [sem(f"qs_in{i}") for i in range(2)]
        s_kv = [sem(f"kv_in{i}") for i in range(2)]
        s_v = [sem(f"values_in{i}") for i in range(2)]
        s_row, s_s, s_exp, s_pv, s_acc, s_l, s_o, s_rec, s_norm = (sem(n) for n in (
            "stack_rows_ready", "scores_ready", "exp_ready", "values_added", "sums_added",
            "denominator_ready", "output_copied", "reciprocal_ready", "output_normal"))
        UN = 2 * KT
        DU = UN - 1
        SPLIT = (2, 5)
        KVB, QSB = 4 * 16, 4 * 16
        SLOTS, PAIRS = 3, NCH // 2
        assert (PAIRS - 2) % SLOTS == 0 and 2 * UN % SLOTS == 1
        OUTB, SUMB = 2 * SLOTS, 2 * SLOTS + 1
        with ExitStack() as s5, nc.Block() as block:
            def sb(name, shape, dt=F32):
                return s5.enter_context(nc.sbuf_tensor(name, shape, dt))

            KS = [sb(f"KS{i}", [P, J, CK], F32R) for i in range(2)]
            QS = [sb(f"QS{i}", [P, J, SQ], F32R) for i in range(2)]
            VC = [sb(f"VC{i}", [P, KT, P]) for i in range(2)]
            PR = [sb(f"PR{i}", [P, 2, SQ]) for i in range(UN)]
            AC = [[sb(f"AC{x}{h}", [P, 2, SQ]) for h in range(2)] for x in range(2)]
            RC = sb("RC", [P, SQ])

            @block.sync
            def _(sp):
                sp.dma_start(WO[:], wo).then_inc(s_wo, 16)
                sp.dma_start(BO[:], bo.partition_broadcast(P)).then_inc(s_wo, 16)
                sp.wait_ge(s_row, 4)
                with sp.Fori(0, B) as b:
                    with sp.Fori(0, G // 2) as gp:
                        for x_ in range(2):
                            g = gp * 2 + x_
                            bg = b * G + gp * 2 + x_
                            sp.wait_ge(s_s, bg * (NCH * UN) + NCH * UN)
                            q = QS[x_]
                            for r, src in ((0, qh_d), (1, qh_d), (2, ql_d)):
                                sp.dma_start(q[r * DH:(r + 1) * DH].bitcast(F32),
                                             src[bg].rearrange("(j d) q -> d j q", j=J)).then_inc(s_qs[x_], 16)
                            sp.dma_start(q[3 * DH:3 * DH + 2].bitcast(F32), shift_d[:, bass.ds(bg * J, J), :]).then_inc(s_qs[x_], 16)
                            with sp.Fori(0, NCH // 2) as i:
                                for s in range(2):
                                    N = bg * NCH + i * 2 + s
                                    n = b * NCH + i * 2 + s
                                    sp.wait_ge(s_s, N * UN + 2 * NCH * UN - UN)
                                    k = KS[s]
                                    for r, src in ((0, kh_d), (1, kl_d), (2, kh_d)):
                                        sp.dma_start(k[r * DH:(r + 1) * DH].bitcast(F32),
                                                     src[n, g].rearrange("(j d) k -> d j k", j=J)).then_inc(s_kv[s], 16)
                                    sp.dma_start(k[3 * DH + 1:3 * DH + 2].bitcast(F32),
                                                 mask_d[n].partition_broadcast(J).unsqueeze(0)).then_inc(s_kv[s], 16)
                                    sp.wait_ge(s_pv, N * UN + UN)
                                    sp.dma_start(VC[s][:], v_d[n, g]).then_inc(s_v[s], 16)

            def chunk_loop(engine, pair):
                with engine.Fori(0, B) as b:
                    with engine.Fori(0, G // 2) as gp:
                        for x_ in range(2):
                            bg = b * G + gp * 2 + x_
                            yield bg, b * (G // 2) + gp, x_
                            pair(bg, x_, 0, True, False, 0)
                            with engine.Fori(0, (PAIRS - 2) // SLOTS) as k:
                                for m in range(1, SLOTS + 1):
                                    pair(bg, x_, k * SLOTS + m, False, False, m)
                            pair(bg, x_, PAIRS - 1, False, True, PAIRS - 1)
                            yield bg, b * (G // 2) + gp, x_

            @block.tensor
            def _(pe):
                def scores(u, s, x_, slot):
                    t, hp = divmod(u, 2)
                    for jj in range(2):
                        j = 2 * hp + jj
                        m = pe.matmul(PS[:, 2 * slot + jj, :], KS[s][:, j, t * P:(t + 1) * P], QS[x_][:, j, :],
                                      start=True, stop=True)
                    m.then_inc(s_s, 1)

                def pair(bg, x_, i, first, last, phase):
                    for s in range(2):
                        N = bg * NCH + i * 2 + s
                        for u in range(UN):
                            slot = (phase + s * UN + u) % SLOTS
                            pe.wait_ge(s_exp, N * UN + u + SLOTS + 1)
                            if u + SLOTS < UN:
                                scores(u + SLOTS, s, x_, slot)
                            elif not (last and s == 1):
                                if u + SLOTS == UN:
                                    pe.wait_ge(s_kv[1 - s], (bg * (NCH // 2) + i + s) * KVB + KVB)
                                scores(u + SLOTS - UN, 1 - s, x_, slot)
                            if u == 0:
                                pe.wait_ge(s_v[s], (bg * (NCH // 2) + i) * 16 + 16)
                                if first and s == 0:
                                    pe.wait_ge(s_o, bg + 1)
                            t, hp = divmod(u, 2)
                            begin, end = first and s == 0, last and s == 1
                            for jj in range(2):
                                j = 2 * hp + jj
                                m = pe.matmul(PS[j * DH:(j + 1) * DH, OUTB, :], VC[s][:, t, j * DH:(j + 1) * DH],
                                              PR[u][:, jj, :], start=begin and t == 0, stop=end and t == KT - 1)
                            if u >= DU or u in SPLIT:
                                if first and s == 0 and u == SPLIT[0]:
                                    pe.wait_ge(s_rec, bg + 1)
                                for jj in ((1,) if u in SPLIT else (0, 1)):
                                    j = 2 * hp + jj
                                    m = pe.matmul(PS[j * DH:(j + 1) * DH, SUMB, :], ones[:], PR[u][:, jj, :],
                                                  start=begin and (u in SPLIT or u == DU and jj == 0), stop=False)
                            m.then_inc(s_pv, 1)

                pe.sem_inc(s_pv, 2 * UN)
                pe.sem_inc(s_s, 2 * NCH * UN)
                begin = True
                for bg, pairs, x_ in chunk_loop(pe, pair):
                    if begin:
                        pe.wait_ge(s_qs[x_], pairs * QSB + QSB)
                        pe.wait_ge(s_kv[0], bg * (NCH // 2 * KVB) + KVB)
                        pe.wait_ge(s_exp, bg * (NCH * UN) + SLOTS)
                        for u in range(SLOTS):
                            scores(u, 0, x_, u)
                    else:
                        pe.wait_ge(s_acc, bg * (NCH * DU) + NCH * DU + DU)
                        for j in range(J):
                            m = pe.matmul(PS[j * DH:(j + 1) * DH, SUMB, :], ones[:], AC[x_][j // 2][:, j % 2, :],
                                          start=j == 0, stop=True)
                        m.then_inc(s_l, 1)
                    begin = not begin

            @block.scalar
            def _(act):
                def pair(bg, x_, i, first, last, phase):
                    for s in range(2):
                        N = bg * NCH + i * 2 + s
                        for u in range(UN):
                            slot = (phase + s * UN + u) % SLOTS
                            act.wait_ge(s_s, N * UN + 2 * NCH * UN + u + 1)
                            act.wait_ge(s_pv, N * UN + UN + u + 1)
                            if u < DU:
                                act.wait_ge(s_acc, N * DU + u + 1)
                            nc.scalar.activation(PR[u][:], PS[:, 2 * slot:2 * slot + 2, :], ACT.Exp,
                                                 scale=SCALE).then_inc(s_exp, 1)

                act.sem_inc(s_exp, SLOTS)
                for _ in chunk_loop(act, pair):
                    pass

            @block.vector
            def _(dve):
                v = nc.vector

                def pair(bg, x_, i, first, last, phase):
                    for s in range(2):
                        N = bg * NCH + i * 2 + s
                        for u in range(DU):
                            dve.wait_ge(s_exp, N * UN + u + SLOTS + 1)
                            a = AC[x_][u % 2]
                            if first and s == 0 and u < 2:
                                v.tensor_copy(a[:], PR[u][:]).then_inc(s_acc, 1)
                            else:
                                dve.wait_ge(s_acc, N * DU + (DU + u - 1 if u else DU))
                                h = 1 if u in SPLIT else 2
                                v.tensor_tensor(a[:, 0:h], a[:, 0:h], PR[u][:, 0:h], ALU.add).then_inc(s_acc, 1)

                for i in range(2):
                    v.memset(KS[i][3 * DH:P].bitcast(F32), 1.0).then_inc(s_row, 1)
                    v.memset(QS[i][3 * DH:P].bitcast(F32), 0.0).then_inc(s_row, 1)
                dve.sem_inc(s_acc, DU)
                dve.sem_inc(s_o, 1)
                dve.sem_inc(s_rec, 1)
                dve.sem_inc(s_norm, 1)
                begin = True
                for bg, pairs, x_ in chunk_loop(dve, pair):
                    if not begin:
                        dve.wait_ge(s_pv, bg * (NCH * UN) + NCH * UN + 2 * UN)
                        v.tensor_copy(AT[:, bg, :], PS[:, OUTB, :]).then_inc(s_o, 1)
                        dve.wait_ge(s_l, bg + 1)
                        dve.wait_ge(s_norm, bg + 1)
                        v.reciprocal(RC[:], PS[:, SUMB, :]).then_inc(s_rec, 1)
                        dve.wait_ge(s_rec, bg + 2)
                        dve.wait_ge(s_o, bg + 2)
                        v.tensor_tensor(AT[:, bg, :], AT[:, bg, :], RC[:], ALU.mult).then_inc(s_norm, 1)
                    begin = not begin
                dve.wait_ge(s_norm, BG + 1)


        NT = 5
        TILEQ = P - 2 * HALF
        STARTS = [i * TILEQ for i in range(NT - 1)] + [SQ - TILEQ]
        EXT = SQ + 2 * HALF
        s_turn, s_turned, s_tok = sem("tile_turned"), sem("tile_turned_out"), sem("tile_normal")

        def turn_tokens(pe, src, bank, k):
            for i in range(TT):
                pe.wait_ge(s_tok, k * TT + i + 1)
                if i >= 2 or k:
                    pe.wait_ge(s_turned, k * TT + i - 1)
                for c in range(DC):
                    m = pe.transpose(PS[:, bank + i % 2, c * P:(c + 1) * P], src[:, i, c * P:(c + 1) * P], ident[:])
                m.then_inc(s_turn, 1)

        def turned_out(act, dst, bank, k):
            for i in range(TT):
                act.wait_ge(s_turn, k * TT + i + 1)
                nc.scalar.activation(dst[:, :, i * P:(i + 1) * P],
                                     PS[:, bank + i % 2, :].rearrange("p (c t) -> p c t", c=DC), ACT.Copy).then_inc(s_turned, 1)

        with six:
            QT = six.enter_context(nc.sbuf_tensor("QT", [P, BG, SQ], F32))
            KE = six.enter_context(nc.sbuf_tensor("KE", [P, BG, EXT], F32))
            VL = six.enter_context(nc.sbuf_tensor("VL", [P, B * NT, D], F32))
            s_w6 = sem("stage6_weights_in")
            s_c6, s_p6, s_x6, s_q6, s_k6, s_kl6, s_klo, s_v6, s_vl6, s_vlo = (sem(n) for n in (
                "dve_chain6", "projected6", "residual6", "qkv_psum6", "qkv_out6", "k_latent_psum", "k_latent_out",
                "v_ext6", "v_latent_psum", "v_latent_out"))
            with ExitStack() as s6, nc.Block() as block:
                def sb(name, shape, dt=F32):
                    return s6.enter_context(nc.sbuf_tensor(name, shape, dt))

                XN, XT = sb("XN6", [P, TT, D]), sb("XT6", [P, DC, T])
                WA, BA = sb("WA", [P, DC, 3 * D]), sb("BA", [P, 3 * G])
                BLr, BLc = sb("BLr", [P, D]), sb("BLc", [P, 1])
                WL = sb("WL", [P, P])
                VE = sb("VE", [P, BG, EXT])
                KPLAIN = sb("KPLAIN", [P, 2, SQ])
                tmp = sb("ln_tmp6", [P, TT, 15])

                @block.sync
                def _(sp):
                    sp.dma_start(WA[:], wqkv).then_inc(s_w6, 16)
                    sp.dma_start(BA[:], bqkv).then_inc(s_w6, 16)
                    sp.wait_ge(s_c6, 1)
                    for j in range(J):
                        sp.dma_start(WL[j * DH:(j + 1) * DH, j * DH:(j + 1) * DH], wlat).then_inc(s_w6, 16)
                        sp.dma_start(BLc[j * DH:(j + 1) * DH, :], blat_c).then_inc(s_w6, 16)
                    for h in range(H):
                        sp.dma_start(BLr[:, h * DH:(h + 1) * DH], blat_r.partition_broadcast(P)).then_inc(s_w6, 16)

                W6 = 16 * (2 + 2 * J + H)

                @block.tensor
                def _(pe):
                    pe.wait_ge(s_wo, 2 * 16)
                    for i in range(TT):
                        b, q = divmod(i, TT // B)
                        if i >= 2:
                            pe.wait_ge(s_x6, i - 1)
                        for g in range(G):
                            m = pe.matmul(PS[:, i % 2, :], AT[:, b * G + g, q * P:(q + 1) * P], WO[:, g, :],
                                          start=(g == 0), stop=(g == G - 1))
                        m.then_inc(s_p6, 1)
                    turn_tokens(pe, XN, 2, 0)
                    pe.wait_ge(s_w6, W6)
                    n = 0
                    for part in range(3):
                        for bg in range(BG):
                            b, g = divmod(bg, G)
                            pe.wait_ge(s_turned, (b + 1) * TT // B)
                            if n >= 2:
                                pe.wait_ge(s_k6, n - 1)
                            for c in range(DC):
                                m = pe.matmul(PS[:, 4 + n % 2, :], WA[:, c, part * D + g * P:part * D + (g + 1) * P],
                                              XT[:, c, b * SQ:(b + 1) * SQ], start=(c == 0), stop=(c == DC - 1))
                            m.then_inc(s_q6, 1)
                            n += 1
                            if part == 1:
                                pe.wait_ge(s_k6, n)
                                if bg >= 2:
                                    pe.wait_ge(s_klo, bg - 1)
                                pe.matmul(PS[:, 6 + bg % 2, :], WL[:], KPLAIN[:, bg % 2, :], start=True, stop=True).then_inc(s_kl6, 1)
                    pe.wait_ge(s_v6, 1)
                    for tile in range(B * NT):
                        b, t = divmod(tile, NT)
                        if tile >= 2:
                            pe.wait_ge(s_vlo, tile - 1)
                        for g in range(G):
                            m = pe.matmul(PS[:, tile % 2, g * P:(g + 1) * P], VE[:, b * G + g, STARTS[t]:STARTS[t] + P], WL[:],
                                          start=True, stop=True)
                        m.then_inc(s_vl6, 1)

                @block.scalar
                def _(act):
                    emit_root(act, tmp, 2)
                    turned_out(act, XT, 2, 0)
                    act.wait_ge(s_w6, W6)
                    for n in range(3 * BG):
                        part, bg = divmod(n, BG)
                        g = bg % G
                        act.wait_ge(s_q6, n + 1)
                        if part == 1 and bg >= 2:
                            act.wait_ge(s_kl6, bg - 1)
                        dst = (QT[:, bg, :], KPLAIN[:, bg % 2, :], VE[:, bg, HALF:HALF + SQ])[part]
                        nc.scalar.activation(dst, PS[:, 4 + n % 2, :], ACT.Identity,
                                             bias=BA[:, part * G + g:part * G + g + 1]).then_inc(s_k6, 1)

                @block.vector
                def _(dve):
                    v = nc.vector
                    chain = Chain(dve, s_c6)
                    chain.mark(v.memset(WL[:], 0.0))
                    dve.wait_ge(s_wo, 2 * 16)
                    for i in range(TT):
                        n = chain.mark(v.tensor_tensor(X[:, i, :], X[:, i, :], BO[:], ALU.add))
                    dve.wait_ge(s_c6, n)
                    for i in range(TT):
                        dve.wait_ge(s_p6, i + 1)
                        v.tensor_tensor(X[:, i, :], X[:, i, :], PS[:, i % 2, :], ALU.add).then_inc(s_x6, 1)
                    dve.wait_ge(s_x6, TT)
                    emit_layernorm(chain, X, XN, tmp, s_tok, 2)
                    dve.wait_ge(s_w6, W6)
                    for bg in range(BG):
                        dve.wait_ge(s_kl6, bg + 1)
                        n = chain.mark(v.tensor_scalar(KE[:, bg, HALF:HALF + SQ], PS[:, 6 + bg % 2, :], BLc[:, 0:1], None, ALU.add))
                        dve.wait_ge(s_c6, n)
                        v.tensor_copy(KE[:, bg, 0:HALF], KE[:, bg, EXT - HALF - 1:EXT - HALF].to_broadcast([P, HALF]))
                        v.tensor_copy(KE[:, bg, EXT - HALF:EXT], KE[:, bg, HALF:HALF + 1].to_broadcast([P, HALF])).then_inc(s_klo, 1)
                    dve.wait_ge(s_k6, 3 * BG)
                    for bg in range(BG):
                        v.tensor_copy(VE[:, bg, 0:HALF], VE[:, bg, EXT - HALF - 1:EXT - HALF].to_broadcast([P, HALF]))
                        m = v.tensor_copy(VE[:, bg, EXT - HALF:EXT], VE[:, bg, HALF:HALF + 1].to_broadcast([P, HALF]))
                    m.then_inc(s_v6, 1)
                    for tile in range(B * NT):
                        dve.wait_ge(s_vl6, tile + 1)
                        v.tensor_tensor(VL[:, tile, :], PS[:, tile % 2, :], BLr[:], ALU.add).then_inc(s_vlo, 1)

            A2 = six.enter_context(nc.sbuf_tensor("A2", [P, DC, T], F32))
            s_wm = sem("window_mask_in")
            s_ws, s_wsm, s_wmx, s_wex, s_wt, s_wev, s_wpv, s_wow, s_wot, s_wo2, s_wr, s_wz = (sem(n) for n in (
                "window_scores", "window_scaled", "window_max", "window_exp", "window_turned", "window_turned_out",
                "window_values", "window_normal", "window_output_turned", "window_output_out",
                "window_reciprocal", "window_sums_zeroed"))
            with ExitStack() as s6, nc.Block() as block:
                def sb(name, shape, dt=F32):
                    return s6.enter_context(nc.sbuf_tensor(name, shape, dt))

                MW = sb("MW", [TILEQ, NT, P])
                SM = [sb(f"SM{i}", [TILEQ, J, G, P]) for i in range(2)]
                PW = [sb(f"PW{i}", [TILEQ, J, G, P]) for i in range(2)]
                PT = [sb(f"PT{i}", [P, J, G, TILEQ]) for i in range(2)]
                OW = [sb(f"OW{i}", [TILEQ, G, J, DH]) for i in range(2)]
                NX, LW, RW = sb("NX", [TILEQ, 2, J * G]), sb("LW", [TILEQ, 2, J * G]), sb("RW", [TILEQ, 2, J * G])
                NW = B * NT

                @block.sync
                def _(sp):
                    sp.dma_start(MW[:], wmask_d).then_inc(s_wm, 16)

                @block.tensor
                def _(pe):
                    def scores(t):
                        b, q = divmod(t, NT)
                        if t >= 1:
                            pe.wait_ge(s_wsm, t)
                        for g in range(G):
                            for j in range(J):
                                r = slice(j * DH, (j + 1) * DH)
                                m = pe.matmul(PS[0:TILEQ, j, g * P:(g + 1) * P], QT[r, b * G + g, STARTS[q]:STARTS[q] + TILEQ],
                                              KE[r, b * G + g, STARTS[q]:STARTS[q] + P], start=True, stop=True)
                        m.then_inc(s_ws, 1)

                    def output(t):
                        pe.wait_ge(s_wow, t + 1)
                        if t >= 1:
                            pe.wait_ge(s_wo2, t)
                        for c in range(DC):
                            m = pe.transpose(PS[:, 6, c * P:c * P + TILEQ], OW[t % 2][:, c].rearrange("p j d -> p (j d)"),
                                             ident[0:TILEQ, 0:TILEQ])
                        m.then_inc(s_wot, 1)

                    scores(0)
                    scores(1)
                    for t in range(NW):
                        pe.wait_ge(s_wex, t + 1)
                        for j in range(J):
                            if j >= 2 or t >= 1:
                                pe.wait_ge(s_wev, J * t + j - 1)
                            for g in range(G):
                                m = pe.transpose(PS[:, 4 + j % 2, g * P:g * P + TILEQ], PW[t % 2][:, j, g, :], ident[0:TILEQ, 0:TILEQ])
                            m.then_inc(s_wt, 1)
                        if t + 2 < NW:
                            scores(t + 2)
                        if t >= 1:
                            output(t - 1)
                        pe.wait_ge(s_wev, J * t + J)
                        for g in range(G):
                            for j in range(J):
                                h = g * J + j
                                m = pe.matmul(PS[0:TILEQ, 7, h * DH:(h + 1) * DH], PT[t % 2][:, j, g, :], VL[:, t, h * DH:(h + 1) * DH],
                                              start=True, stop=True)
                        m.then_inc(s_wpv, 1)
                    output(NW - 1)

                @block.scalar
                def _(act):
                    act.wait_ge(s_wz, 1)
                    for t in range(NW):
                        act.wait_ge(s_wmx, t + 1)
                        if t >= 2:
                            act.wait_ge(s_wt, (t - 1) * J)
                            act.wait_ge(s_wr, t - 1)
                        for j in range(J):
                            for g in range(G):
                                k = j * G + g
                                m = nc.scalar.activation(PW[t % 2][:, j, g, :], SM[t % 2][:, j, g, :], ACT.Exp,
                                                         bias=NX[:, t % 2, k:k + 1], accum_out=LW[:, t % 2, k:k + 1])
                        m.then_inc(s_wex, 1)

                @block.vector
                def _(dve):
                    v = nc.vector

                    def scale(t):
                        dve.wait_ge(s_ws, t + 1)
                        if t >= 2:
                            dve.wait_ge(s_wex, t - 1)
                        v.scalar_tensor_tensor(SM[t % 2][:].rearrange("p j g k -> p (j g) k"),
                                               PS[0:TILEQ, 0:J, :].rearrange("p j (g k) -> p (j g) k", g=G), SCALE,
                                               MW[:, t % NT, :].unsqueeze(1).to_broadcast([TILEQ, J * G, P]),
                                               ALU.mult, ALU.add).then_inc(s_wsm, 1)
                        dve.wait_ge(s_wsm, t + 1)
                        v.tensor_reduce(NX[:, t % 2, :], SM[t % 2][:].rearrange("p j g k -> p (j g) k"), AX.X, ALU.max,
                                        negate=True).then_inc(s_wmx, 1)

                    def turned(t):
                        b, q = divmod(t, NT)
                        dve.wait_ge(s_wot, t + 1)
                        v.tensor_copy(A2[:, :, b * SQ + STARTS[q]:b * SQ + STARTS[q] + TILEQ],
                                      PS[:, 6, :].rearrange("p (c q) -> p c q", c=DC)[:, :, 0:TILEQ]).then_inc(s_wo2, 1)

                    v.memset(LW[:], 0.0).then_inc(s_wz, 1)
                    dve.wait_ge(s_wm, 16)
                    scale(0)
                    scale(1)
                    for t in range(NW):
                        for j in range(J):
                            dve.wait_ge(s_wt, t * J + j + 1)
                            if t >= 2 and j == 0:
                                dve.wait_ge(s_wpv, t - 1)
                            v.tensor_copy(PT[t % 2][:, j], PS[:, 4 + j % 2, :].rearrange("p (g q) -> p g q", g=G)[:, :, 0:TILEQ]
                                          ).then_inc(s_wev, 1)
                        if t + 2 < NW:
                            scale(t + 2)
                        v.reciprocal(RW[:, t % 2, :], LW[:, t % 2, :]).then_inc(s_wr, 1)
                        dve.wait_ge(s_wr, t + 1)
                        if t >= 1:
                            turned(t - 1)
                        dve.wait_ge(s_wpv, t + 1)
                        v.tensor_tensor(OW[t % 2][:], PS[0:TILEQ, 7, :].rearrange("p (g j d) -> p g j d", g=G, j=J),
                                        RW[:, t % 2, :].rearrange("p (j g) -> p g j", j=J).unsqueeze(3).to_broadcast([TILEQ, G, J, DH]),
                                        ALU.mult).then_inc(s_wow, 1)
                    turned(NW - 1)


            XT7 = AT[:].rearrange("p (c b) q -> p c (b q)", c=DC)
            h_d = dram("h_d", [T, D], F32)
            s_w8, s_c8, s_p8, s_x8, s_h8 = (sem(n) for n in (
                "projection_in", "dve_chain8", "window_projected", "residual8", "tokens_stored"))
            with ExitStack() as s6, nc.Block() as block:
                XN = s6.enter_context(nc.sbuf_tensor("XN8", [P, TT, D], F32))
                WP = s6.enter_context(nc.sbuf_tensor("WP", [P, DC, D], F32))
                BP = s6.enter_context(nc.sbuf_tensor("BP", [P, D], F32))
                tmp = s6.enter_context(nc.sbuf_tensor("ln_tmp8", [P, TT, 15], F32))

                @block.sync
                def _(sp):
                    sp.dma_start(WP[:], wproj).then_inc(s_w8, 16)
                    sp.dma_start(BP[:], bproj.partition_broadcast(P)).then_inc(s_w8, 16)
                    sp.wait_ge(s_tok, 2 * TT)
                    sp.dma_start(h_d.rearrange("(i p) d -> p i d", p=P), XN[:]).then_inc(s_h8, 16)
                    sp.wait_ge(s_h8, 16)

                @block.tensor
                def _(pe):
                    pe.wait_ge(s_w8, 32)
                    for i in range(TT):
                        if i >= 2:
                            pe.wait_ge(s_x8, i - 1)
                        for c in range(DC):
                            m = pe.matmul(PS[:, i % 2, :], A2[:, c, i * P:(i + 1) * P], WP[:, c, :],
                                          start=(c == 0), stop=(c == DC - 1))
                        m.then_inc(s_p8, 1)
                    turn_tokens(pe, XN, 2, 1)

                @block.scalar
                def _(act):
                    emit_root(act, tmp, 3)
                    turned_out(act, XT7, 2, 1)

                @block.vector
                def _(dve):
                    v = nc.vector
                    chain = Chain(dve, s_c8)
                    dve.wait_ge(s_w8, 32)
                    for i in range(TT):
                        n = chain.mark(v.tensor_tensor(X[:, i, :], X[:, i, :], BP[:], ALU.add))
                    dve.wait_ge(s_c8, n)
                    for i in range(TT):
                        dve.wait_ge(s_p8, i + 1)
                        v.tensor_tensor(X[:, i, :], X[:, i, :], PS[:, i % 2, :], ALU.add).then_inc(s_x8, 1)
                    dve.wait_ge(s_x8, TT)
                    emit_layernorm(chain, X, XN, tmp, s_tok, 3)

        FC = 4
        FT = FF // FC // P
        WU = [st.enter_context(nc.sbuf_tensor(f"WU{k}", [P, DC, FF // FC], F32)) for k in range(FC)]
        WG = [st.enter_context(nc.sbuf_tensor(f"WG{k}", [P, DC, FF // FC], F32)) for k in range(FC)]
        WD = [st.enter_context(nc.sbuf_tensor(f"WD{k}", [P, FT, D], F32)) for k in range(FC)]
        score = st.enter_context(nc.sbuf_tensor("score", [CAP, E], F32))
        token = st.enter_context(nc.sbuf_tensor("token", [CAP, E], U32))
        s_ex = [sem(f"expert_weights_in{k}") for k in range(FC)]
        s_sw, s_gw = [sem(f"shared_weights_in{i}") for i in range(2)], sem("gate_weights_in")
        s_gl, s_gs, s_c9, s_tk, s_tt, s_to = (sem(n) for n in (
            "gate_logits", "gate_scores", "topk_chain", "topk_ready", "topk_turned", "topk_out"))
        s_su, s_sg, s_sh, s_sd, s_so, s_out = (sem(n) for n in (
            "shared_products", "shared_silu", "shared_hidden", "shared_down", "shared_added", "base_stored"))
        HFS = SH // 2
        HTURN = HFS // P

        def load_step(sp, e, k):
            sp.dma_start(WU[k][:], up_w[e, k]).then_inc(s_ex[k], 16)
            sp.dma_start(WG[k][:], gw[e, k]).then_inc(s_ex[k], 16)
            sp.dma_start(WD[k][:], down_w[e, k]).then_inc(s_ex[k], 16)

        with ExitStack() as s7, nc.Block() as block:
            def sb(name, shape, dt=F32):
                return s7.enter_context(nc.sbuf_tensor(name, shape, dt))

            SG = [sb(f"SG{i}", [P, DC, HFS]) for i in range(2)]
            SU = [sb(f"SU{i}", [P, DC, HFS]) for i in range(2)]
            SD = [sb(f"SD{i}", [P, HTURN, D]) for i in range(2)]
            HS = sb("HS", [P, HTURN, SQ])
            SL = [sb(f"SL{i}", [P, SQ]) for i in range(2)]
            GW = sb("GW", [P, DC, E])
            GS = [sb(f"GS{i}", [E, T]) for i in range(2)]
            TV, TI, TF = sb("TV", [E, CAP]), sb("TI", [E, CAP], U32), sb("TF", [E, CAP])
            ROUNDS = CAP // 8

            @block.sync
            def _(sp):
                sp.dma_start(GW[:], gate_w).then_inc(s_gw, 16)
                for i in range(2):
                    sp.dma_start(SG[i][:], sh_gate[:, :, i * HFS:(i + 1) * HFS]).then_inc(s_sw[i], 16)
                    sp.dma_start(SU[i][:], sh_up[:, :, i * HFS:(i + 1) * HFS]).then_inc(s_sw[i], 16)
                    sp.dma_start(SD[i][:], sh_down[:, i * HTURN:(i + 1) * HTURN, :]).then_inc(s_sw[i], 16)
                for k in range(FC):
                    load_step(sp, 0, k)
                for i in range(TT):
                    sp.wait_ge(s_so, TT + i + 1)
                    sp.dma_start(out[i * P:(i + 1) * P, :], X[:, i, :]).then_inc(s_out, 16)
                sp.wait_ge(s_out, 16 * TT)

            @block.tensor
            def _(pe):
                pe.wait_ge(s_gw, 16)
                for b in range(B):
                    for c in range(DC):
                        m = pe.matmul(PS[0:E, 6 + b, :], GW[:, c, :], XT7[:, c, b * SQ:(b + 1) * SQ],
                                      start=(c == 0), stop=(c == DC - 1))
                m.then_inc(s_gl, 1)
                for n in range(2 * B):
                    i, b = divmod(n, B)
                    if b == 0:
                        pe.wait_ge(s_sw[i], 48)
                    for f in range(HTURN):
                        q = n * HTURN + f
                        if q >= 2:
                            pe.wait_ge(s_sh, q - 1)
                        for w, bank in ((SG, 0), (SU, 2)):
                            for c in range(DC):
                                m = pe.matmul(PS[:, bank + q % 2, :], w[i][:, c, f * P:(f + 1) * P],
                                              XT7[:, c, b * SQ:(b + 1) * SQ], start=(c == 0), stop=(c == DC - 1))
                        m.then_inc(s_su, 1)
                    pe.wait_ge(s_sh, n * HTURN + HTURN)
                    for t in range(TT // B):
                        q = n * (TT // B) + t
                        if q >= 2:
                            pe.wait_ge(s_so, q - 1)
                        for f in range(HTURN):
                            m = pe.matmul(PS[:, 4 + q % 2, :], HS[:, f, t * P:(t + 1) * P], SD[i][:, f, :],
                                          start=(f == 0), stop=(f == HTURN - 1))
                        m.then_inc(s_sd, 1)
                pe.wait_ge(s_tk, 1)
                pe.transpose(PS[:, 6, 0:E], TV[:], ident[0:E, 0:E])
                pe.transpose(PS[:, 6, E:2 * E], TF[:], ident[0:E, 0:E]).then_inc(s_tt, 1)

            @block.scalar
            def _(act):
                act.wait_ge(s_gl, 1)
                for b in range(B):
                    m = nc.scalar.activation(GS[0][:, b * SQ:(b + 1) * SQ], PS[0:E, 6 + b, :], ACT.Sigmoid)
                m.then_inc(s_gs, 1)
                for q in range(2 * B * HTURN):
                    act.wait_ge(s_su, q + 1)
                    if q >= 2:
                        act.wait_ge(s_sh, q - 1)
                    nc.scalar.activation(SL[q % 2][:], PS[:, q % 2, :], ACT.Silu).then_inc(s_sg, 1)

            @block.vector
            def _(dve):
                v = nc.vector
                chain = Chain(dve, s_c9)

                def topk_round(r):
                    a, b = GS[r % 2], GS[1 - r % 2]
                    s8 = slice(8 * r, 8 * r + 8)
                    chain.link(v.max(TV[:, s8], a[:]))
                    chain.mark(v.max_index(TI[:, s8], TV[:, s8], a[:]))
                    chain.link(v.match_replace(b[:], TV[:, s8], a[:], -1.0))

                def hidden(q):
                    n, f = divmod(q, HTURN)
                    dve.wait_ge(s_sg, q + 1)
                    if f == 0 and n >= 1:
                        dve.wait_ge(s_sd, n * (TT // B))
                    v.tensor_tensor(HS[:, f, :], PS[:, 2 + q % 2, :], SL[q % 2][:], ALU.mult).then_inc(s_sh, 1)

                def add_down(q):
                    i, t = divmod(q, TT)
                    dve.wait_ge(s_sd, q + 1)
                    if i >= 1:
                        dve.wait_ge(s_so, t + 1)
                    v.tensor_tensor(X[:, t, :], X[:, t, :], PS[:, 4 + q % 2, :], ALU.add).then_inc(s_so, 1)

                dve.wait_ge(s_gs, 1)
                rounds = 0
                for n in range(2 * B):
                    for f in range(HTURN):
                        hidden(n * HTURN + f)
                        if rounds < ROUNDS:
                            topk_round(rounds)
                            rounds += 1
                    for t in range(TT // B):
                        add_down(n * (TT // B) + t)
                while rounds < ROUNDS:
                    topk_round(rounds)
                    rounds += 1
                v.tensor_copy(TF[:], TI[:]).then_inc(s_tk, 1)
                dve.wait_ge(s_tt, 1)
                v.tensor_copy(score[:], PS[:, 6, 0:E]).then_inc(s_to, 1)
                v.tensor_copy(token[:], PS[:, 6, E:2 * E]).then_inc(s_to, 1)

        s_ga, s_bi, s_db = sem("tokens_gathered"), sem("expert_biases_in"), [sem(f"down_bias_in{i}") for i in range(2)]
        s_xf, s_xt, s_xo, s_pu, s_si, s_hi, s_dn, s_y, s_yb, s_sc = (sem(n) for n in (
            "expert_rows", "expert_rows_turned", "expert_rows_out", "expert_products", "expert_silu", "expert_hidden",
            "expert_step_down", "expert_output", "expert_biased", "expert_scattered"))
        s_fr, s_g0 = sem("output_slot_free"), sem("first_gathered")
        with ExitStack() as s7, nc.Block() as block:
            def sb(name, shape, dt=F32):
                return s7.enter_context(nc.sbuf_tensor(name, shape, dt))

            XG = sb("XG", [CAP, E, D])
            XF = [sb(f"XF{i}", [CAP, D]) for i in range(2)]
            XE = [sb(f"XE{i}", [P, DC, CAP]) for i in range(2)]
            UB, GB = sb("UB", [P, E, FF // P]), sb("GB", [P, E, FF // P])
            DB = [sb(f"DB{i}", [P, D]) for i in range(2)]
            YB = [sb(f"YB{i}", [P, D]) for i in range(2)]
            YO = [sb(f"YO{i}", [P, D]) for i in range(2)]
            SE = [sb(f"SE{i}", [P, FT, CAP]) for i in range(2)]
            HE = [sb(f"HE{i}", [P, FT, CAP]) for i in range(2)]
            ST = E * FC

            @block.sync
            def _(sp):
                sp.dma_start(UB[:], up_b).then_inc(s_bi, 16)
                sp.dma_start(GB[:], gb).then_inc(s_bi, 16)
                for x_ in range(2):
                    sp.dma_start(DB[x_][:], down_b[x_].partition_broadcast(P)).then_inc(s_db[x_], 16)

                def refill(e, k):
                    sp.wait_ge(s_dn, e * FC + k - FC + 3)
                    load_step(sp, e, k)

                with sp.Fori(0, E // 2 - 1) as i:
                    for x_ in range(2):
                        for k in range(FC):
                            refill(i * 2 + x_ + 1, k)
                        sp.wait_ge(s_yb, i * 2 + x_ + 3)
                        sp.dma_start(DB[x_][:], down_b[i * 2 + x_ + 2].partition_broadcast(P)).then_inc(s_db[x_], 16)
                for k in range(FC):
                    refill(E - 1, k)

            @block.gpsimd
            def _(pool):
                pool.sem_inc(s_fr, 2)
                pool.wait_ge(s_to, 2)
                for e in range(E):
                    nc.gpsimd.indirect_dma_start(XG[:, e, :], None, h_d, bass.IndirectOffsetOnAxis(ap=token[:, e:e + 1], axis=0)
                                                 ).then_inc(s_ga if e else s_g0, 16)
                for e in range(E):
                    pool.wait_ge(s_y, e + 1)
                    if e:
                        pool.wait_ge(s_sc, 16 * e)
                        pool.sem_inc(s_fr, 1)
                    nc.gpsimd.indirect_dma_start(out, bass.IndirectOffsetOnAxis(ap=token[:, e:e + 1], axis=0), YO[e % 2][:], None,
                                                 compute_op=ALU.add).then_inc(s_sc, 16)
                pool.wait_ge(s_sc, 16 * E)

            @block.tensor
            def _(pe):
                def turn(e, x_):
                    pe.wait_ge(s_xf, e + 1)
                    pe.wait_ge(s_xo, e + 1)
                    for c in range(DC):
                        m = pe.transpose(PS[:, 6, c * P:(c + 1) * P], XF[x_][:, c * P:(c + 1) * P], ident[:])
                    m.then_inc(s_xt, 1)

                def up(e, x_, k):
                    S = e * FC + k
                    pe.wait_ge(s_ex[k], e * 48 + 48)
                    if k == 0:
                        pe.wait_ge(s_xo, e + 2)
                    pe.wait_ge(s_hi, S + 1)
                    for w, bank in ((WG, 0), (WU, 2)):
                        for f in range(FT):
                            for c in range(DC):
                                m = pe.matmul(PS[:, bank + k % 2, f * P:(f + 1) * P], w[k][:, c, f * P:(f + 1) * P],
                                              XE[x_][:, c, :], start=(c == 0), stop=(c == DC - 1))
                        m.then_inc(s_pu, 1)

                def down(e, x_, k):
                    S = e * FC + k
                    pe.wait_ge(s_hi, S + 3)
                    if k == 0:
                        pe.wait_ge(s_yb, e + 1)
                    for f in range(FT):
                        m = pe.matmul(PS[:, 4 + x_, :], HE[k % 2][:, f, :], WD[k][:, f, :],
                                      start=(k == 0 and f == 0), stop=(k == FC - 1 and f == FT - 1))
                    m.then_inc(s_dn, 1)

                def expert(e, x_, last=False):
                    for k in range(FC):
                        if k + 1 < FC:
                            up(e, x_, k + 1)
                        elif not last:
                            up(e + 1, 1 - x_, 0)
                        down(e, x_, k)
                        if k == 1 and not last:
                            turn(e + 1, 1 - x_)

                pe.sem_inc(s_dn, 2)
                turn(0, 0)
                up(0, 0, 0)
                with pe.Fori(0, E // 2 - 1) as i:
                    for x_ in range(2):
                        expert(i * 2 + x_, x_)
                expert(E - 2, 0)
                expert(E - 1, 1, last=True)

            @block.scalar
            def _(act):
                act.wait_ge(s_bi, 32)
                with act.Fori(0, E // 2) as i:
                    for x_ in range(2):
                        e = i * 2 + x_
                        for k in range(FC):
                            S = e * FC + k
                            act.wait_ge(s_pu, S * 2 + 1)
                            act.wait_ge(s_hi, S + 1)
                            for f in range(FT):
                                m = nc.scalar.activation(SE[k % 2][:, f, :], PS[:, k % 2, f * P:(f + 1) * P], ACT.Silu,
                                                         bias=GB[:, e, k * FT + f:k * FT + f + 1])
                            m.then_inc(s_si, 1)

            @block.vector
            def _(dve):
                v = nc.vector

                def rows(e, x_):
                    v.tensor_copy(XF[x_][:], XG[:, e, :]).then_inc(s_xf, 1)

                def rows_out(e, x_):
                    dve.wait_ge(s_xt, e + 1)
                    v.tensor_copy(XE[x_][:], PS[:, 6, :].rearrange("p (c t) -> p c t", c=DC)).then_inc(s_xo, 1)

                def expert(e, i, x_, last=False):
                    for k in range(FC):
                        S = e * FC + k
                        dve.wait_ge(s_si, S + 1)
                        dve.wait_ge(s_pu, S * 2 + 2)
                        dve.wait_ge(s_dn, S + 1)
                        for f in range(FT):
                            m = v.scalar_tensor_tensor(HE[k % 2][:, f, :], PS[:, 2 + k % 2, f * P:(f + 1) * P],
                                                       UB[:, e, k * FT + f:k * FT + f + 1], SE[k % 2][:, f, :],
                                                       ALU.add, ALU.mult)
                        m.then_inc(s_hi, 1)
                        if k == 0 and not last:
                            rows(e + 1, 1 - x_)
                        if k == 1 and not last:
                            rows_out(e + 1, 1 - x_)
                    dve.wait_ge(s_dn, e * FC + FC + 2)
                    dve.wait_ge(s_db[x_], i * 16 + 16)
                    v.tensor_tensor(YB[x_][:], PS[:, 4 + x_, :], DB[x_][:], ALU.add).then_inc(s_yb, 1)
                    dve.wait_ge(s_yb, e + 3)
                    dve.wait_ge(s_fr, e + 1)
                    v.tensor_scalar(YO[x_][:], YB[x_][:], score[:, bass.ds(e, 1)], None, ALU.mult).then_inc(s_y, 1)

                dve.sem_inc(s_hi, 2)
                dve.sem_inc(s_yb, 2)
                dve.sem_inc(s_xo, 1)
                dve.wait_ge(s_bi, 32)
                dve.wait_ge(s_g0, 16)
                rows(0, 0)
                rows_out(0, 0)
                dve.wait_ge(s_ga, 16 * (E - 1))
                with dve.Fori(0, E // 2 - 1) as i:
                    for x_ in range(2):
                        expert(i * 2 + x_, i, x_)
                expert(E - 2, E // 2 - 1, 0)
                expert(E - 1, E // 2 - 1, 1, last=True)


def by_contraction(w):
    n, k = w.shape
    return np.ascontiguousarray(w.T.reshape(k // P, P, n).transpose(1, 0, 2))


def by_partition(b):
    return np.ascontiguousarray(b.reshape(-1, P).T)


def window_mask():
    wq = P - 2 * HALF
    starts = [0, wq, 2 * wq, 3 * wq, SQ - wq]
    query = np.array(starts)[None, :, None] + np.arange(wq)[:, None, None]
    key = np.array(starts)[None, :, None] - HALF + np.arange(P)[None, None, :]
    times = ((key >= 0) & (key < SQ) & (np.abs(key - query) <= HALF)).astype(np.float64)
    times = np.where(key == -1, np.maximum(HALF - query, 0), times)
    times = np.where(key == SQ, np.maximum(query - (SQ - 1 - HALF), 0), times)
    return np.where(times > 0, np.log(np.maximum(times, 1)), MASKED).astype(np.float32)


def kernel(**inputs):
    import concourse.bacc as bacc
    from concourse.bass_utils import run_bass_kernel_spmd

    a = {k: np.asarray(v) for k, v in inputs.items()}
    fs = FF // 4
    laid = {
        "x": a["x"].reshape(T, D),
        "ctx": np.ascontiguousarray(a["ctx_1024"].reshape(B * NCH, CK, DC, P).transpose(0, 3, 2, 1)),
        "mask": a["mask_Bx1x1xS2_if1"].reshape(B * NCH, CK),
        "wq": by_contraction(a["L0_xattn_Wq"]), "bq": by_partition(a["L0_xattn_bq"]),
        "wk": by_contraction(a["L0_xattn_Wk"]), "bk": by_partition(a["L0_xattn_bk"]),
        "wv": by_contraction(a["L0_xattn_Wv"]), "bv": a["L0_xattn_bv"],
        "ident": np.eye(P, dtype=np.float32),
        "blocks": np.kron(np.eye(J), np.ones((DH, DH))).astype(np.float32),
        "wo": by_contraction(a["L0_xattn_Wo"]), "bo": a["L0_xattn_bo"],
        "wqkv": by_contraction(a["L0_attn_W_qkv"]), "bqkv": by_partition(a["L0_attn_b_qkv"]),
        "wlat": np.ascontiguousarray(a["L0_attn_W_lat"].T), "blat_c": a["L0_attn_b_lat"].reshape(DH, 1),
        "blat_r": a["L0_attn_b_lat"], "wmask": window_mask(),
        "wproj": by_contraction(a["L0_attn_W_proj"]), "bproj": a["L0_attn_b_proj"],
        "gate_w": by_contraction(a["L0_ffn_gate_w"]),
        "up_w": np.ascontiguousarray(a["L0_ffn_up_w"].reshape(E, 4, fs, DC, P).transpose(0, 1, 4, 3, 2)),
        "up_b": np.ascontiguousarray(a["L0_ffn_up_b"].reshape(E, FF // P, P).transpose(2, 0, 1)),
        "gw": np.ascontiguousarray(a["L0_ffn_gw"].reshape(E, 4, fs, DC, P).transpose(0, 1, 4, 3, 2)),
        "gb": np.ascontiguousarray(a["L0_ffn_gb"].reshape(E, FF // P, P).transpose(2, 0, 1)),
        "down_w": np.ascontiguousarray(a["L0_ffn_down_w"].reshape(E, D, 4, fs // P, P).transpose(0, 2, 4, 3, 1)),
        "down_b": a["L0_ffn_down_b"],
        "sh_gate": by_contraction(a["L0_ffn_sh_gate_w"]), "sh_up": by_contraction(a["L0_ffn_sh_up_w"]),
        "sh_down": by_contraction(a["L0_ffn_sh_down_w"]),
    }
    nc = bacc.Bacc("TRN2", target_bir_lowering=False, num_devices=1)
    arrays, args = {}, []
    for name, value in laid.items():
        arrays[f"in_{name}"] = value
        args.append(nc.dram_tensor(f"in_{name}", value.shape, mybir.dt.from_np(value.dtype), kind="ExternalInput").ap())
    out = nc.dram_tensor("out_0", (T, D), F32, kind="ExternalOutput").ap()
    program(nc, *args, out)
    r = run_bass_kernel_spmd(nc, [arrays], core_ids=[0])
    return r.results[0]["out_0"].reshape(B, SQ, D)
```
